# Optimizing a Trainium2 kernel written in Bass

```python
import numpy as np
import jax
import jax.numpy as jnp

def _softmax(x, axis=-1):
    return jax.nn.softmax(x, axis=axis)

def _gelu(x):
    return jax.nn.gelu(x, approximate=True)

def _silu(x):
    return jax.nn.silu(x)

def _sigmoid(x):
    return jax.nn.sigmoid(x)

def _layernorm(x, axis=-1, eps=1e-05):
    m = jnp.mean(x, axis=axis, keepdims=True)
    v = jnp.var(x, axis=axis, keepdims=True)
    return (x - m) / jnp.sqrt(v + eps)

def _scatter_add(tgt, idx, src, axis=0):
    return tgt.at[idx].add(src)

def _segment_sum(src, seg, n):
    return jax.ops.segment_sum(src, seg, n)
kernel_name = 'mk_dlrm_tower_d1_rec_r8_107fd1'

def setup_inputs(seed: int=0):
    np.random.seed(seed)
    _w = jnp.asarray

    def _rec_inputs():
        import jax
        import jax.numpy as jnp
        _tk = jax.random.key(seed)
        dense_ctx = jax.random.normal(jax.random.fold_in(_tk, 190), (2048, 16), jnp.float32)
        ids = jnp.stack([jax.random.randint(jax.random.fold_in(_tk, 200 + f), (2048,), 0, v, jnp.int32) for f, v in enumerate([125000, 1250, 1000, 1000, 1000, 1000, 1250, 1250, 1250, 1000, 1000, 1250, 1000, 125000, 12500, 1250, 1250, 12500, 125000, 1000, 1250, 1000, 12500, 12500, 1250, 1250, 1000, 1250, 1250, 1250, 1250, 1250, 12500, 1250, 1000, 1250, 1000, 12500, 12500])], axis=1)
        tbl_0 = 0.05 * jax.random.normal(jax.random.fold_in(_tk, 500 + 0), (125000, 64), jnp.float32)
        tbl_1 = 0.05 * jax.random.normal(jax.random.fold_in(_tk, 500 + 1), (1250, 64), jnp.float32)
        tbl_2 = 0.05 * jax.random.normal(jax.random.fold_in(_tk, 500 + 2), (1000, 64), jnp.float32)
        tbl_3 = 0.05 * jax.random.normal(jax.random.fold_in(_tk, 500 + 3), (1000, 64), jnp.float32)
        tbl_4 = 0.05 * jax.random.normal(jax.random.fold_in(_tk, 500 + 4), (1000, 64), jnp.float32)
        tbl_5 = 0.05 * jax.random.normal(jax.random.fold_in(_tk, 500 + 5), (1000, 64), jnp.float32)
        tbl_6 = 0.05 * jax.random.normal(jax.random.fold_in(_tk, 500 + 6), (1250, 64), jnp.float32)
        tbl_7 = 0.05 * jax.random.normal(jax.random.fold_in(_tk, 500 + 7), (1250, 64), jnp.float32)
        tbl_8 = 0.05 * jax.random.normal(jax.random.fold_in(_tk, 500 + 8), (1250, 64), jnp.float32)
        tbl_9 = 0.05 * jax.random.normal(jax.random.fold_in(_tk, 500 + 9), (1000, 64), jnp.float32)
        tbl_10 = 0.05 * jax.random.normal(jax.random.fold_in(_tk, 500 + 10), (1000, 64), jnp.float32)
        tbl_11 = 0.05 * jax.random.normal(jax.random.fold_in(_tk, 500 + 11), (1250, 64), jnp.float32)
        tbl_12 = 0.05 * jax.random.normal(jax.random.fold_in(_tk, 500 + 12), (1000, 64), jnp.float32)
        tbl_13 = 0.05 * jax.random.normal(jax.random.fold_in(_tk, 500 + 13), (125000, 64), jnp.float32)
        tbl_14 = 0.05 * jax.random.normal(jax.random.fold_in(_tk, 500 + 14), (12500, 64), jnp.float32)
        tbl_15 = 0.05 * jax.random.normal(jax.random.fold_in(_tk, 500 + 15), (1250, 64), jnp.float32)
        tbl_16 = 0.05 * jax.random.normal(jax.random.fold_in(_tk, 500 + 16), (1250, 64), jnp.float32)
        tbl_17 = 0.05 * jax.random.normal(jax.random.fold_in(_tk, 500 + 17), (12500, 64), jnp.float32)
        tbl_18 = 0.05 * jax.random.normal(jax.random.fold_in(_tk, 500 + 18), (125000, 64), jnp.float32)
        tbl_19 = 0.05 * jax.random.normal(jax.random.fold_in(_tk, 500 + 19), (1000, 64), jnp.float32)
        tbl_20 = 0.05 * jax.random.normal(jax.random.fold_in(_tk, 500 + 20), (1250, 64), jnp.float32)
        tbl_21 = 0.05 * jax.random.normal(jax.random.fold_in(_tk, 500 + 21), (1000, 64), jnp.float32)
        tbl_22 = 0.05 * jax.random.normal(jax.random.fold_in(_tk, 500 + 22), (12500, 64), jnp.float32)
        tbl_23 = 0.05 * jax.random.normal(jax.random.fold_in(_tk, 500 + 23), (12500, 64), jnp.float32)
        tbl_24 = 0.05 * jax.random.normal(jax.random.fold_in(_tk, 500 + 24), (1250, 64), jnp.float32)
        tbl_25 = 0.05 * jax.random.normal(jax.random.fold_in(_tk, 500 + 25), (1250, 64), jnp.float32)
        tbl_26 = 0.05 * jax.random.normal(jax.random.fold_in(_tk, 500 + 26), (1000, 64), jnp.float32)
        tbl_27 = 0.05 * jax.random.normal(jax.random.fold_in(_tk, 500 + 27), (1250, 64), jnp.float32)
        tbl_28 = 0.05 * jax.random.normal(jax.random.fold_in(_tk, 500 + 28), (1250, 64), jnp.float32)
        tbl_29 = 0.05 * jax.random.normal(jax.random.fold_in(_tk, 500 + 29), (1250, 64), jnp.float32)
        tbl_30 = 0.05 * jax.random.normal(jax.random.fold_in(_tk, 500 + 30), (1250, 64), jnp.float32)
        tbl_31 = 0.05 * jax.random.normal(jax.random.fold_in(_tk, 500 + 31), (1250, 64), jnp.float32)
        tbl_32 = 0.05 * jax.random.normal(jax.random.fold_in(_tk, 500 + 32), (12500, 64), jnp.float32)
        tbl_33 = 0.05 * jax.random.normal(jax.random.fold_in(_tk, 500 + 33), (1250, 64), jnp.float32)
        tbl_34 = 0.05 * jax.random.normal(jax.random.fold_in(_tk, 500 + 34), (1000, 64), jnp.float32)
        tbl_35 = 0.05 * jax.random.normal(jax.random.fold_in(_tk, 500 + 35), (1250, 64), jnp.float32)
        tbl_36 = 0.05 * jax.random.normal(jax.random.fold_in(_tk, 500 + 36), (1000, 64), jnp.float32)
        tbl_37 = 0.05 * jax.random.normal(jax.random.fold_in(_tk, 500 + 37), (12500, 64), jnp.float32)
        tbl_38 = 0.05 * jax.random.normal(jax.random.fold_in(_tk, 500 + 38), (12500, 64), jnp.float32)
        _rk = jax.random.fold_in(_tk, 7)
        W_top1 = 0.0833333 * jax.random.normal(jax.random.fold_in(_tk, 801), (144, 512), jnp.float32)
        W_top2 = 0.0441942 * jax.random.normal(jax.random.fold_in(_tk, 802), (512, 256), jnp.float32)
        W_top3 = 0.0625 * jax.random.normal(jax.random.fold_in(_tk, 803), (256, 1), jnp.float32)
        b_top1 = jnp.zeros((512,), jnp.float32)
        b_top2 = jnp.zeros((256,), jnp.float32)
        return (dense_ctx, ids, tbl_0, tbl_1, tbl_2, tbl_3, tbl_4, tbl_5, tbl_6, tbl_7, tbl_8, tbl_9, tbl_10, tbl_11, tbl_12, tbl_13, tbl_14, tbl_15, tbl_16, tbl_17, tbl_18, tbl_19, tbl_20, tbl_21, tbl_22, tbl_23, tbl_24, tbl_25, tbl_26, tbl_27, tbl_28, tbl_29, tbl_30, tbl_31, tbl_32, tbl_33, tbl_34, tbl_35, tbl_36, tbl_37, tbl_38, W_top1, b_top1, W_top2, b_top2, W_top3)
    dense_ctx, ids, tbl_0, tbl_1, tbl_2, tbl_3, tbl_4, tbl_5, tbl_6, tbl_7, tbl_8, tbl_9, tbl_10, tbl_11, tbl_12, tbl_13, tbl_14, tbl_15, tbl_16, tbl_17, tbl_18, tbl_19, tbl_20, tbl_21, tbl_22, tbl_23, tbl_24, tbl_25, tbl_26, tbl_27, tbl_28, tbl_29, tbl_30, tbl_31, tbl_32, tbl_33, tbl_34, tbl_35, tbl_36, tbl_37, tbl_38, W_top1, b_top1, W_top2, b_top2, W_top3 = _rec_inputs()

    def _L0_rec_setup():
        import jax, jax.numpy as jnp
        import numpy as np
        B, F, E, UNITS = (1024, 39, 64, 128)
        key = jax.random.key(seed)
        k1, k2 = jax.random.split(key)
        embeds = jax.random.normal(k1, (B, F, E), dtype=jnp.float32)
        inner_w = jax.random.normal(k2, (UNITS, F), dtype=jnp.float32) * (2.0 / (UNITS + F)) ** 0.5
        return {'embeds': embeds, 'inner_w': inner_w}
    _L0_rec_all = _L0_rec_setup()
    _L0_rec_in = {k: v for k, v in _L0_rec_all.items() if k in ('inner_w',)}
    del _L0_rec_all
    return {'dense_ctx': dense_ctx, 'ids': ids, 'tbl_0': tbl_0, 'tbl_1': tbl_1, 'tbl_2': tbl_2, 'tbl_3': tbl_3, 'tbl_4': tbl_4, 'tbl_5': tbl_5, 'tbl_6': tbl_6, 'tbl_7': tbl_7, 'tbl_8': tbl_8, 'tbl_9': tbl_9, 'tbl_10': tbl_10, 'tbl_11': tbl_11, 'tbl_12': tbl_12, 'tbl_13': tbl_13, 'tbl_14': tbl_14, 'tbl_15': tbl_15, 'tbl_16': tbl_16, 'tbl_17': tbl_17, 'tbl_18': tbl_18, 'tbl_19': tbl_19, 'tbl_20': tbl_20, 'tbl_21': tbl_21, 'tbl_22': tbl_22, 'tbl_23': tbl_23, 'tbl_24': tbl_24, 'tbl_25': tbl_25, 'tbl_26': tbl_26, 'tbl_27': tbl_27, 'tbl_28': tbl_28, 'tbl_29': tbl_29, 'tbl_30': tbl_30, 'tbl_31': tbl_31, 'tbl_32': tbl_32, 'tbl_33': tbl_33, 'tbl_34': tbl_34, 'tbl_35': tbl_35, 'tbl_36': tbl_36, 'tbl_37': tbl_37, 'tbl_38': tbl_38, 'W_top1': W_top1, 'b_top1': b_top1, 'W_top2': W_top2, 'b_top2': b_top2, 'W_top3': W_top3, 'L0_rec_inner_w': _L0_rec_in['inner_w']}

def reference(dense_ctx, ids, tbl_0, tbl_1, tbl_2, tbl_3, tbl_4, tbl_5, tbl_6, tbl_7, tbl_8, tbl_9, tbl_10, tbl_11, tbl_12, tbl_13, tbl_14, tbl_15, tbl_16, tbl_17, tbl_18, tbl_19, tbl_20, tbl_21, tbl_22, tbl_23, tbl_24, tbl_25, tbl_26, tbl_27, tbl_28, tbl_29, tbl_30, tbl_31, tbl_32, tbl_33, tbl_34, tbl_35, tbl_36, tbl_37, tbl_38, W_top1, b_top1, W_top2, b_top2, W_top3, L0_rec_inner_w):
    import jax
    import jax.numpy as jnp

    def _L0_rec_ref(embeds, inner_w):
        import jax, jax.numpy as jnp
        import numpy as np
        B, F, E, UNITS = (1024, 39, 64, 128)
        delta = jnp.einsum('uf,bfe->bue', inner_w, embeds)
        lp = jnp.sum(delta * delta, axis=-1)
        return lp
    e = jnp.stack([tbl_0[ids[:, 0]], tbl_1[ids[:, 1]], tbl_2[ids[:, 2]], tbl_3[ids[:, 3]], tbl_4[ids[:, 4]], tbl_5[ids[:, 5]], tbl_6[ids[:, 6]], tbl_7[ids[:, 7]], tbl_8[ids[:, 8]], tbl_9[ids[:, 9]], tbl_10[ids[:, 10]], tbl_11[ids[:, 11]], tbl_12[ids[:, 12]], tbl_13[ids[:, 13]], tbl_14[ids[:, 14]], tbl_15[ids[:, 15]], tbl_16[ids[:, 16]], tbl_17[ids[:, 17]], tbl_18[ids[:, 18]], tbl_19[ids[:, 19]], tbl_20[ids[:, 20]], tbl_21[ids[:, 21]], tbl_22[ids[:, 22]], tbl_23[ids[:, 23]], tbl_24[ids[:, 24]], tbl_25[ids[:, 25]], tbl_26[ids[:, 26]], tbl_27[ids[:, 27]], tbl_28[ids[:, 28]], tbl_29[ids[:, 29]], tbl_30[ids[:, 30]], tbl_31[ids[:, 31]], tbl_32[ids[:, 32]], tbl_33[ids[:, 33]], tbl_34[ids[:, 34]], tbl_35[ids[:, 35]], tbl_36[ids[:, 36]], tbl_37[ids[:, 37]], tbl_38[ids[:, 38]]], axis=1)
    z = _L0_rec_ref(e, L0_rec_inner_w)
    z = z.reshape(z.shape[0], -1)
    h = jnp.concatenate([z, dense_ctx], axis=1)
    h = jnp.maximum(h @ W_top1 + b_top1, 0.0)
    h = jnp.maximum(h @ W_top2 + b_top2, 0.0)
    y = h @ W_top3
    return y

_drawn_inputs = setup_inputs


def setup_inputs(seed=0):
    import zlib

    import numpy as np

    out = dict(_drawn_inputs(seed))
    spreads = {'b_top1': (0.0, 0.344), 'b_top2': (0.0, 0.1)}
    factors = {'tbl_0': 7.667,
     'tbl_1': 6.316,
     'tbl_2': 7.191,
     'tbl_3': 8.0,
     'tbl_4': 6.245,
     'tbl_5': 7.473,
     'tbl_6': 6.799,
     'tbl_7': 6.71,
     'tbl_8': 6.822,
     'tbl_9': 7.213,
     'tbl_10': 6.627,
     'tbl_11': 7.554,
     'tbl_12': 7.503,
     'tbl_13': 8.0,
     'tbl_14': 7.05,
     'tbl_15': 6.046,
     'tbl_16': 6.225,
     'tbl_17': 7.23,
     'tbl_18': 6.545,
     'tbl_19': 8.0,
     'tbl_20': 6.564,
     'tbl_21': 7.459,
     'tbl_22': 6.405,
     'tbl_23': 6.855,
     'tbl_24': 6.506,
     'tbl_25': 7.432,
     'tbl_26': 6.481,
     'tbl_27': 5.987,
     'tbl_28': 7.94,
     'tbl_29': 6.66,
     'tbl_30': 8.0,
     'tbl_31': 6.829,
     'tbl_32': 7.129,
     'tbl_33': 6.942,
     'tbl_34': 6.631,
     'tbl_35': 7.569,
     'tbl_36': 6.833,
     'tbl_37': 7.87,
     'tbl_38': 7.973}
    for name, (base, spread) in spreads.items():
        noise = np.random.default_rng([zlib.crc32(name.encode()), seed]).standard_normal(out[name].shape)
        drawn = base * np.exp(spread * noise) if base else spread * noise
        out[name] = jnp.asarray(drawn.astype(out[name].dtype))
    for name, factor in factors.items():
        out[name] = (out[name] * factor).astype(out[name].dtype)
    return out
```

```python
from contextlib import ExitStack

import concourse.bass as bass
import numpy as np
from concourse import mybir

F32 = mybir.dt.float32
BF16 = mybir.dt.bfloat16
F16 = mybir.dt.float16
I32 = mybir.dt.int32
ALU = mybir.AluOpType
ACT = mybir.ActivationFunctionType
AX = mybir.AxisListType

P = 128
B, F, E, U = 2048, 39, 64, 128
D, H1, H2 = 16, 512, 256
TB = 128
NB = 2 * TB
STEPS = B // NB

ROWS = 1000
CH = 8
KP = ROWS // CH
N_ONEHOT = 12
PAIRS = N_ONEHOT // 2
PARTS = 3

J = 3
EG = 22
PITCH = J * EG
KT = J * F
UNITS = EG // 2
ORDER = [(g // 2, g % 2, j) for g in range(EG) for j in range(J) if g + EG * j < E]
QUADS = len(ORDER) // 4
FIRST_OF_UNIT = [min(n for n, o in enumerate(ORDER) if o[0] == u) for u in range(UNITS)] + [E]
SQ = 3
OHR = 3

JOBS = [
    (1, "look", (0, 0)), (1, "look", (0, 1)), (2, "mlp", 0),
    (3, "look", (1, 0)), (3, "look", (1, 1)), (4, "mlp", 1),
    (5, "look", (2, 0)), (5, "look", (2, 1)), (6, "mlp", 2),
    (7, "look", (3, 0)), (7, "look", (3, 1)), (8, "mlp", 3),
    (9, "look", (4, 0)), (9, "look", (4, 1)),
    (10, "look", (5, 0)), (10, "look", (5, 1)),
]
LOOKS = 2 * PAIRS
MLP_READS = [2, 4, 6, 7]
MLPS = MLP_READS[-1]


def build(nc, tables, ids, ids_by_field, dense_t, w_t, w1, b1, w2, b2, w3, out):
    with ExitStack() as ctx:
        def sb(name, shape, dt):
            return ctx.enter_context(nc.sbuf_tensor(name, shape, dt))

        def pb(name, shape, dt):
            return ctx.enter_context(nc.psum_tensor(name, shape, dt))

        def sem(name):
            return ctx.enter_context(nc.semaphore(name))

        x = [sb(f"x{k}", [P, F * PITCH], F32) for k in range(4)]
        x_slots = [t[:, :].rearrange("p (f c) -> p f c", c=PITCH) for t in x]
        idx = [sb(f"idx{k}", [P, F], I32) for k in range(4)]
        idb = sb("idb", [KP, N_ONEHOT, NB], I32)
        idh = [sb(f"idh{k}", [KP, N_ONEHOT, NB], F16) for k in range(2)]
        onehot = [sb(f"onehot{k}", [KP, CH, 2, NB], BF16) for k in range(OHR)]
        shared = sb("shared", [P, max(N_ONEHOT * CH * E, UNITS * 2 * NB)], F32)
        stage = shared[0:KP, 0:N_ONEHOT * CH * E].rearrange("p (f c e) -> p f c e", f=N_ONEHOT, c=CH)
        xt = shared[0:KT, 0:UNITS * 2 * NB].rearrange("p (u g b) -> p u g b", u=UNITS, g=2)
        table = sb("table", [KP, N_ONEHOT, CH, PARTS, E], BF16)
        row_no = sb("row_no", [KP, CH], F32)
        wj = [sb(f"wj{j}", [KT, U], F32) for j in range(J)]
        ident = sb("ident", [P, P], F32)
        ones = sb("ones", [P, P], F32)
        sq = [sb(f"sq{k}", [P, 4 * NB], F32) for k in range(SQ)]
        acc = [sb(f"acc{k}", [P, 4 * NB], F32) for k in range(2)]
        z = [sb(f"z{k}", [P, NB], F32) for k in range(2)]
        dense = sb("dense", [P, B], F32)
        w1z = sb("w1z", [P, H1], F32)
        w1d = sb("w1d", [P, H1], F32)
        w2s = sb("w2s", [P, H1 // P, H2], F32)
        w3s = sb("w3s", [P, H2 // P], F32)
        b1s = sb("b1s", [P, H1 // P], F32)
        b2s = sb("b2s", [P, H2 // P], F32)
        h1 = sb("h1", [P, H1 // P, NB], F32)
        h2 = sb("h2", [P, H2 // P, NB], F32)
        y = sb("y", [1, B], F32)

        delta = [pb(f"delta{k}", [P, 4 * NB], F32) for k in range(2)]
        turned = [pb(f"turned{k}", [P, 2, 2, TB], F32) for k in range(2)]
        side = [pb(f"side{k}", [P, 512], F32) for k in range(2)]

        idx_in = [sem(f"idx_in{k}") for k in range(4)]
        gathered = [sem(f"gathered{k}") for k in range(4)]
        idb_in = sem("idb_in")
        tables_in = [sem(f"tables_in{k}") for k in range(PAIRS)]
        wj_in = sem("wj_in")
        mlp_in = sem("mlp_in")
        stored = sem("stored")
        pads_zero = sem("pads_zero")
        ones_set = sem("ones_set")
        wj_zero = sem("wj_zero")
        dense_zero = sem("dense_zero")
        ident_set = sem("ident_set")
        rows_set = sem("rows_set")
        part1 = sem("part1")
        rest1 = sem("rest1")
        part2 = sem("part2")
        split = sem("split")
        cast = sem("cast")
        hot = sem("hot")
        looked = sem("looked")
        filled = sem("filled")
        turned_up = sem("turned_up")
        xt_ready = sem("xt_ready")
        projected = sem("projected")
        squared = sem("squared")
        summed = sem("summed")
        z_ready = sem("z_ready")
        mlp_done = sem("mlp_done")
        mlp_read = sem("mlp_read")

        GATHERS = F - N_ONEHOT
        at_units = lambda s: s * UNITS
        at_quads = lambda s: s * QUADS
        at_sums = lambda s: s * (QUADS - 1)
        at_looks = lambda s: (s + 1) * LOOKS
        at_pairs = lambda s: (s + 1) * PAIRS
        at_mlps = lambda s: (s - 1) * 4
        at_reads = lambda s: (s - 1) * MLPS

        def wait(eng, semaphore, value):
            if not isinstance(value, int) or value > 0:
                eng.wait_ge(semaphore, value)

        def supersteps(eng, step, first, last):
            assert (last - first) % 2 == 1
            with eng.Fori(0, (last - first + 1) // 2) as i:
                for k in range(2):
                    step(i * 2 + (first + k), (first + k) % 2)

        with nc.Block() as block:

            @block.sync
            def _(sp):
                def load_idx(s, k):
                    sp.dma_start(idx[k][:, :], ids[bass.ds((s * 2 + k % 2) * TB, TB), :]).then_inc(idx_in[k], 16)

                def load_idb(s):
                    src = ids_by_field[:, bass.ds(s * NB, NB)]
                    sp.dma_start(idb[:, :, :], src.partition_broadcast(KP)).then_inc(idb_in, 16)

                load_idx(0, 0)
                load_idx(0, 1)
                load_idb(0)
                for k in range(PAIRS):
                    for q in (2 * k, 2 * k + 1):
                        sp.dma_start(stage[:, q, :, :], tables[q].rearrange("(p c) e -> p c e", c=CH)).then_inc(tables_in[k], 16)
                load_idx(1, 2)
                load_idx(1, 3)
                sp.wait_ge(cast, 2)
                load_idb(1)
                sp.wait_ge(wj_zero, J)
                for j in range(J):
                    sp.dma_start(wj[j][j:KT:J, :], w_t).then_inc(wj_in, 16)
                sp.dma_start(w1z[:, :], w1[0:P, :]).then_inc(mlp_in, 16)
                sp.wait_ge(dense_zero, 2)
                sp.dma_start(w1d[0:D, :], w1[P:P + D, :]).then_inc(mlp_in, 16)
                sp.dma_start(dense[0:D, :], dense_t).then_inc(mlp_in, 16)
                sp.dma_start(w2s[:, :, :], w2.rearrange("(k p) n -> p k n", p=P)).then_inc(mlp_in, 16)
                with nc.allow_non_contiguous_dma(reason="small vectors, once"):
                    sp.dma_start(w3s[:, :], w3.rearrange("(k p) o -> p (k o)", p=P)).then_inc(mlp_in, 16)
                    sp.dma_start(b1s[:, :], b1.rearrange("(k p) -> p k", p=P)).then_inc(mlp_in, 16)
                    sp.dma_start(b2s[:, :], b2.rearrange("(k p) -> p k", p=P)).then_inc(mlp_in, 16)

                def step(s, p):
                    for k in (2 * p, 2 * p + 1):
                        sp.wait_ge(gathered[k], (s - p) * (8 * GATHERS))
                        load_idx(s, k)
                    sp.wait_ge(cast, s * 2)
                    load_idb(s)

                supersteps(sp, step, 2, STEPS - 1)
                sp.wait_ge(mlp_read, at_reads(STEPS + 1))
                sp.dma_start(out.rearrange("b o -> o b"), y[:, :]).then_inc(stored, 16)
                sp.wait_ge(stored, 16)

            @block.gpsimd
            def _(pool):
                def gather(s, p, first=False):
                    if not first:
                        pool.wait_ge(turned_up, at_units(s - 1))
                    for k in (2 * p, 2 * p + 1):
                        pool.wait_ge(idx_in[k], 16 if first else s * 8 + (16 - 8 * p))
                        if not first:
                            pool.nop(nofuse=True)
                        for f in range(N_ONEHOT, F):
                            pool.indirect_dma_start(
                                x_slots[k][:, f, 0:E], None, tables[f],
                                bass.IndirectOffsetOnAxis(idx[k][:, f:f + 1], 0),
                            ).then_inc(gathered[k], 16)

                pool.iota(row_no[:, :], [[1, CH]], base=0, channel_multiplier=CH,
                          allow_small_or_imprecise_dtypes=True).then_inc(rows_set, 1)
                pool.wait_ge(ones_set, 1)
                pool.affine_select(ident[:, :], ones[:, :], [[-1, P]], ALU.is_equal, 0.0,
                                   base=0, channel_multiplier=1).then_inc(ident_set, 1)
                gather(0, 0, first=True)
                gather(1, 1, first=True)
                supersteps(pool, gather, 2, STEPS - 1)

            @block.tensor
            def _(pe):
                def free_bank(s, n):
                    known = isinstance(s, int)
                    for back in range(3):
                        for m in reversed(range(n if back == 0 else len(JOBS))):
                            kind, what = JOBS[m][1:]
                            there = not known or (s - back >= 1 if kind == "mlp" else -1 <= s - back < STEPS - 1)
                            if m % 2 == n % 2 and there:
                                if kind == "look":
                                    pe.wait_ge(filled, at_looks(s - back) + 2 * what[0] + what[1] + 1)
                                else:
                                    pe.wait_ge(mlp_read, at_reads(s - back) + MLP_READS[what])
                                return

                def look_up(s, n, k, h):
                    free_bank(s, n)
                    if h == 0:
                        pe.wait_ge(hot, at_pairs(s) + k + 1)
                    if isinstance(s, int) and s == -1 and h == 0:
                        pe.wait_ge(split, k + 1)
                    for q in range(2):
                        for c in range(CH):
                            mm = pe.matmul(side[n % 2][:, q * PARTS * E:(q + 1) * PARTS * E],
                                           onehot[k % OHR][:, c, q, h * TB:(h + 1) * TB],
                                           table[:, 2 * k + q, c, :, :].rearrange("p r e -> p (r e)"),
                                           start=c == 0, stop=c == CH - 1)
                    mm.then_inc(looked, 1)

                def mlp(s, n, part, p):
                    if part == 0:
                        pe.wait_ge(z_ready, s)
                    else:
                        pe.wait_ge(mlp_read, at_reads(s) + MLP_READS[part - 1])
                    free_bank(s, n)
                    bank = side[n % 2]
                    if part < 2:
                        for m in range(2):
                            cols = slice((2 * part + m) * P, (2 * part + m + 1) * P)
                            o = bank[:, m * NB:(m + 1) * NB]
                            pe.matmul(o, w1z[:, cols], z[1 - p][:, :], start=True, stop=False)
                            mm = pe.matmul(o, w1d[:, cols], dense[:, bass.ds((s - 1) * NB, NB)],
                                           start=False, stop=True)
                    elif part == 2:
                        for m in range(2):
                            for k in range(H1 // P):
                                mm = pe.matmul(bank[:, m * NB:(m + 1) * NB], w2s[:, k, m * P:(m + 1) * P],
                                               h1[:, k, :], start=k == 0, stop=k == H1 // P - 1)
                    else:
                        for k in range(H2 // P):
                            mm = pe.matmul(bank[0:1, 0:NB], w3s[:, k:k + 1], h2[:, k, :],
                                           start=k == 0, stop=k == H2 // P - 1)
                    mm.then_inc(mlp_done, 1)

                def transpose(s, u, p):
                    if u == 0:
                        for k in (2 * p, 2 * p + 1):
                            pe.wait_ge(gathered[k], (s - p) * (8 * GATHERS) + 16 * GATHERS)
                        pe.wait_ge(filled, at_looks(s))
                    wait(pe, xt_ready, at_units(s) + (u - 1 if u >= 2 else 0))
                    for g in range(2):
                        for h in range(2):
                            e0 = 2 * u + g
                            mm = pe.transpose(turned[u % 2][0:KT, g, h, :], x[2 * p + h][:, e0:e0 + EG * (KT - 1) + 1:EG],
                                              ident[:, :])
                    mm.then_inc(turned_up, 1)

                def project(s, u):
                    pe.wait_ge(xt_ready, at_units(s) + u + 1)
                    for n in range(FIRST_OF_UNIT[u], FIRST_OF_UNIT[u + 1]):
                        _, g, j = ORDER[n]
                        quad = n // 4
                        if n % 4 == 0:
                            wait(pe, squared, at_quads(s) + quad - 1)
                        mm = pe.matmul(delta[quad % 2][:, (n % 4) * NB:(n % 4 + 1) * NB], wj[j][:, :],
                                       xt[:, u, g, :], start=True, stop=True)
                        if n % 4 == 3:
                            mm.then_inc(projected, 1)

                def step(s, p, look=True, run_mlp=True):
                    transpose(s, 0, p)
                    for u in range(UNITS):
                        if u + 1 < UNITS:
                            transpose(s, u + 1, p)
                        project(s, u)
                        for n, (at, kind, what) in enumerate(JOBS):
                            if at == u and kind == "look" and look:
                                look_up(s, n, *what)
                            if at == u and kind == "mlp" and run_mlp:
                                mlp(s, n, what, p)

                pe.wait_ge(pads_zero, 4)
                pe.wait_ge(ident_set, 1)
                for n, (_, kind, what) in enumerate(JOBS):
                    if kind == "look":
                        look_up(-1, n, *what)
                pe.wait_ge(wj_in, 16 * J)
                step(0, 0, run_mlp=False)
                pe.wait_ge(mlp_in, 16 * 7)
                supersteps(pe, step, 1, STEPS - 2)
                step(STEPS - 1, 1, look=False)
                for n, (_, kind, what) in enumerate(JOBS):
                    if kind == "mlp":
                        mlp(STEPS, n, what, 0)

            @block.scalar
            def _(act):
                def cast_ids(s, p, half):
                    cols = slice(0, 4) if half == 0 else slice(4, N_ONEHOT)
                    if half == 0:
                        act.wait_ge(idb_in, s * 16 + 16)
                        wait(act, hot, at_pairs(s - 2))
                    act.activation(idh[p][:, cols, :], idb[:, cols, :], ACT.Copy).then_inc(cast, 1)

                def copy_turned(s, u):
                    act.wait_ge(turned_up, at_units(s) + u + 1)
                    wait(act, projected, at_quads(s - 1) + (FIRST_OF_UNIT[u + 1] - 1) // 4 + 1)
                    act.activation(xt[:, u, :, :], turned[u % 2][0:KT, :, :, :].rearrange("p g h b -> p g (h b)"),
                                   ACT.Copy).then_inc(xt_ready, 1)

                def square(s, quad, p):
                    act.wait_ge(projected, at_quads(s) + quad + 1)
                    if quad == 0:
                        to = acc[p]
                    else:
                        wait(act, summed, at_sums(s) + quad - 1 - (SQ - 1))
                        to = sq[(quad - 1) % SQ]
                    act.activation(to[:, :], delta[quad % 2][:, :], ACT.Square).then_inc(squared, 1)

                def read_mlp(s, n, part):
                    act.wait_ge(mlp_done, at_mlps(s) + part + 1)
                    bank = side[n % 2]
                    if part < 3:
                        to, bias = ((h1, b1s), (h1, b1s), (h2, b2s))[part]
                        for m in range(2):
                            k = 2 * part + m if part < 2 else m
                            act.activation(to[:, k, :], bank[:, m * NB:(m + 1) * NB], ACT.Relu,
                                           bias=bias[:, k:k + 1]).then_inc(mlp_read, 1)
                    else:
                        act.activation(y[:, bass.ds((s - 1) * NB, NB)], bank[0:1, 0:NB], ACT.Copy).then_inc(mlp_read, 1)

                def step(s, p, look=True, run_mlp=True):
                    copy_turned(s, 0)
                    if look:
                        cast_ids(s + 1, 1 - p, 0)
                    for u in range(UNITS):
                        if u + 1 < UNITS:
                            copy_turned(s, u + 1)
                        if u == 0 and look:
                            cast_ids(s + 1, 1 - p, 1)
                        for quad in range(QUADS):
                            if FIRST_OF_UNIT[u] <= 4 * quad + 3 < FIRST_OF_UNIT[u + 1]:
                                square(s, quad, p)
                        for n, (at, kind, what) in enumerate(JOBS):
                            if at == u and kind == "mlp" and run_mlp:
                                read_mlp(s, n, what)

                cast_ids(0, 0, 0)
                cast_ids(0, 0, 1)
                for k in range(PAIRS):
                    pair = slice(2 * k, 2 * k + 2)
                    act.wait_ge(tables_in[k], 32)
                    act.activation(table[:, pair, :, 0, :], stage[:, pair, :, :], ACT.Copy).then_inc(part1, 1)
                    if k:
                        pair = slice(2 * k - 2, 2 * k)
                        act.wait_ge(rest1, k)
                        act.activation(table[:, pair, :, 1, :], stage[:, pair, :, :], ACT.Copy).then_inc(part2, 1)
                act.wait_ge(rest1, PAIRS)
                act.activation(table[:, N_ONEHOT - 2:N_ONEHOT, :, 1, :], stage[:, N_ONEHOT - 2:N_ONEHOT, :, :],
                               ACT.Copy).then_inc(part2, 1)
                step(0, 0, run_mlp=False)
                act.wait_ge(mlp_in, 16 * 7)
                supersteps(act, step, 1, STEPS - 2)
                step(STEPS - 1, 1, look=False)
                for n, (_, kind, what) in enumerate(JOBS):
                    if kind == "mlp":
                        read_mlp(STEPS, n, what)

            @block.vector
            def _(dve):
                def make_hot(s, k, p):
                    dve.wait_ge(cast, (s + 1) * 2 + (1 if 2 * k + 2 <= 4 else 2))
                    wait(dve, looked, at_looks(s) + 2 * (k - OHR) + 2)
                    for c in range(CH):
                        ins = dve.tensor_scalar(onehot[k % OHR][:, c, :, :], idh[p][:, 2 * k:2 * k + 2, :],
                                                row_no[:, c:c + 1], None, ALU.is_equal)
                    ins.then_inc(hot, 1)

                def fill(s, n, k, h, p):
                    dve.wait_ge(looked, at_looks(s) + 2 * k + h + 1)
                    parts = side[n % 2][:, 0:2 * PARTS * E].rearrange("p (q r e) -> p q e r", q=2, r=PARTS)
                    dve.tensor_reduce(x_slots[2 * p + h][:, 2 * k:2 * k + 2, 0:E], parts, AX.X, ALU.add).then_inc(filled, 1)

                def add(s, quad, p):
                    if quad == 0:
                        return
                    dve.wait_ge(squared, at_quads(s) + quad + 1)
                    if quad > 1:
                        dve.wait_ge(summed, at_sums(s) + quad - 1)
                    dve.tensor_tensor(acc[p][:, :], acc[p][:, :], sq[(quad - 1) % SQ][:, :], ALU.add).then_inc(summed, 1)
                    if quad == QUADS - 1:
                        dve.wait_ge(summed, at_sums(s) + quad)
                        dve.tensor_reduce(z[p][:, :], acc[p][:, :].rearrange("p (e b) -> p b e", e=4), AX.X,
                                          ALU.add).then_inc(z_ready, 1)

                def step(s, p, look=True):
                    if look:
                        make_hot(s, 0, 1 - p)
                        make_hot(s, 1, 1 - p)
                    for u in range(UNITS):
                        for quad in range(QUADS):
                            if FIRST_OF_UNIT[u] <= 4 * quad + 3 < FIRST_OF_UNIT[u + 1]:
                                add(s, quad, p)
                        for n, (at, kind, what) in enumerate(JOBS):
                            if at == u and kind == "look" and look:
                                k, h = what
                                fill(s, n, k, h, 1 - p)
                                if h == 1 and k + 2 < PAIRS:
                                    make_hot(s, k + 2, 1 - p)

                dve.memset(ones[:, :], 1.0).then_inc(ones_set, 1)
                for j in range(J):
                    dve.memset(wj[j][:, :], 0.0).then_inc(wj_zero, 1)
                for t in x_slots:
                    dve.memset(t[:, :, E:PITCH], 0.0).then_inc(pads_zero, 1)
                dve.memset(w1d[:, :], 0.0).then_inc(dense_zero, 1)
                dve.memset(dense[:, :], 0.0).then_inc(dense_zero, 1)
                dve.wait_ge(rows_set, 1)
                make_hot(-1, 0, 0)
                make_hot(-1, 1, 0)
                for k in range(PAIRS + 1):
                    if k < PAIRS:
                        pair = slice(2 * k, 2 * k + 2)
                        dve.wait_ge(part1, k + 1)
                        dve.tensor_tensor(stage[:, pair, :, :], stage[:, pair, :, :], table[:, pair, :, 0, :],
                                          ALU.subtract).then_inc(rest1, 1)
                    if k:
                        pair = slice(2 * k - 2, 2 * k)
                        dve.wait_ge(part2, k)
                        dve.tensor_tensor(table[:, pair, :, 2, :], stage[:, pair, :, :], table[:, pair, :, 1, :],
                                          ALU.subtract).then_inc(split, 1)
                for n, (_, kind, what) in enumerate(JOBS):
                    if kind == "look":
                        k, h = what
                        fill(-1, n, k, h, 0)
                        if h == 1 and k + 2 < PAIRS:
                            make_hot(-1, k + 2, 0)
                step(0, 0)
                supersteps(dve, step, 1, STEPS - 2)
                step(STEPS - 1, 1, look=False)


def kernel(**inputs):
    import concourse.bacc as bacc
    from concourse.bass_utils import run_bass_kernel_spmd as run

    nc = bacc.Bacc("TRN2", target_bir_lowering=False, num_devices=1)
    arrays = {}

    def put(name, a):
        a = np.ascontiguousarray(a)
        arrays[name] = a
        return nc.dram_tensor(name, a.shape, mybir.dt.from_np(a.dtype), kind="ExternalInput").ap()

    small = [f for f in range(F) if inputs[f"tbl_{f}"].shape[0] == ROWS][:N_ONEHOT]
    slots = small + [f for f in range(F) if f not in small]
    ids = np.asarray(inputs["ids"])
    tables = [put(f"tbl_{f}", inputs[f"tbl_{f}"]) for f in slots]
    args = [
        put("ids", ids[:, slots]),
        put("ids_by_field", ids[:, small].T),
        put("dense_t", np.asarray(inputs["dense_ctx"]).T),
        put("w_t", np.asarray(inputs["L0_rec_inner_w"])[:, slots].T),
    ]
    args += [put(n, inputs[n]) for n in ("W_top1", "b_top1", "W_top2", "b_top2", "W_top3")]
    out = nc.dram_tensor("out", (B, 1), F32, kind="ExternalOutput").ap()
    build(nc, tables, *args, out)
    r = run(nc, [arrays], core_ids=[0])
    return r.results[0]["out"]
```

```python
from contextlib import ExitStack

import concourse.bass as bass
import numpy as np
from concourse import mybir

F32 = mybir.dt.float32
BF16 = mybir.dt.bfloat16
F16 = mybir.dt.float16
F32R = mybir.dt.float32r
I32 = mybir.dt.int32
ALU = mybir.AluOpType
ACT = mybir.ActivationFunctionType
AX = mybir.AxisListType

P = 128
B, F, E, U = 2048, 39, 64, 128
D, H1, H2 = 16, 512, 256
TB = 128
NB = 2 * TB
STEPS = B // NB

KP = 125
PAIR_CH = [8] * 6 + [10]
PAIR_Q = [2] * 6 + [1]
PAIRS = len(PAIR_CH)
N_ONEHOT = sum(PAIR_Q)
MAX_CH = max(PAIR_CH)
PARTS = 3

J = 3
EG = 22
PITCH = J * EG
KT = J * F
UNITS = EG // 2
ORDER = [(g // 2, g % 2, j) for g in range(EG) for j in range(J) if g + EG * j < E]
QUADS = len(ORDER) // 4
FIRST_OF_UNIT = [min(n for n, o in enumerate(ORDER) if o[0] == u) for u in range(UNITS)] + [E]
QUADS_OF_UNIT = {u: [q for q in range(QUADS) if ORDER[4 * q + 3][0] == u] for u in range(-1, UNITS)}
XR = 4
SQ = 3
LAST_IN_RING = lambda n, ring, k: max(m for m in range(n) if m % ring == k)
OHR = 3
STAGES = 4

JOBS = [
    ("look", (0, 0), -0.9), ("look", (0, 1), -0.8), ("mlp", 0, 2), ("look", (1, 0), 3), ("look", (1, 1), 4),
    ("mlp", 1, 5), ("look", (2, 0), 6), ("look", (2, 1), 7), ("look", (3, 0), 8), ("mlp", 2, 9),
    ("look", (3, 1), 10), ("look", (4, 0), 11), ("look", (4, 1), 12), ("mlp", 3, 13), ("look", (5, 0), 14),
    ("look", (5, 1), 15), ("look", (6, 0), 16), ("look", (6, 1), 17),
]
assert len(JOBS) % 2 == 0
TURN_AT = [-2, -1.5] + [2 * u - 4 for u in range(2, UNITS)]
QUAD_AT = [2 * ORDER[4 * q + 3][0] + ORDER[4 * q + 3][1] for q in range(QUADS)]
HOT_AT = [at - 2.5 for kind, what, at in JOBS if kind == "look" and what[1] == 0]
HOT_AT = [at if at >= -2 else at + EG for at in HOT_AT]
EARLY = [k for k in range(PAIRS) if HOT_AT[k] > HOT_AT[-1]]
ADD_LAG = 1.2
CAST_AT = max(HOT_AT[k] for k in range(PAIRS) if k not in EARLY) + 1


def timetable(*rows):
    return [call for _, call in sorted(((at, call) for at, call in rows), key=lambda row: row[0])]


LOOKS = 2 * PAIRS
MLP_READS = [2, 4, 6, 7]
MLPS = MLP_READS[-1]


def build(nc, tables, ids, ids_by_field, dense_t, w_t, w1, b1, w2, b2, w3, out):
    with ExitStack() as ctx:
        def sb(name, shape, dt):
            return ctx.enter_context(nc.sbuf_tensor(name, shape, dt))

        def pb(name, shape, dt):
            return ctx.enter_context(nc.psum_tensor(name, shape, dt))

        def sem(name):
            return ctx.enter_context(nc.semaphore(name))

        x_all = sb("x_all", [P, 4, F * PITCH], F32)
        x = [x_all[:, k, :] for k in range(4)]
        x_slots = [t.rearrange("p (f c) -> p f c", c=PITCH) for t in x]
        stage = [x_all[0:KP, 2:4, :].rearrange("p k c -> p (k c)")[:, k * 2 * MAX_CH * E:][:, 0:q * ch * E]
                 .rearrange("p (q c e) -> p q c e", q=q, c=ch)
                 for k, ch, q in [(n % STAGES, ch, PAIR_Q[n]) for n, ch in enumerate(PAIR_CH)]]
        idx = [sb(f"idx{k}", [P, F], I32) for k in range(4)]
        idb = sb("idb", [KP, N_ONEHOT, NB], I32)
        idh = sb("idh", [KP, N_ONEHOT, NB], F16)
        onehot = [sb(f"onehot{k}", [KP, MAX_CH, 2, NB], BF16) for k in range(OHR)]
        table = [sb(f"table{k}", [KP, PAIR_Q[k], ch, PARTS, E], BF16) for k, ch in enumerate(PAIR_CH)]
        row_no = {ch: sb(f"row_no{ch}", [KP, ch], F32) for ch in sorted(set(PAIR_CH))}
        xh = sb("xh", [KT, XR, 2, NB], F32R)
        xl = sb("xl", [KT, XR, 2, NB], F32R)
        wj = [sb(f"wj{j}", [KT, U], F32) for j in range(J)]
        wjh = [sb(f"wjh{j}", [KT, U], F32R) for j in range(J)]
        wjl = [sb(f"wjl{j}", [KT, U], F32R) for j in range(J)]
        ident = sb("ident", [P, P], F32)
        ones = sb("ones", [P, P], F32)
        sq = [sb(f"sq{k}", [P, 4 * NB], F32) for k in range(SQ)]
        acc_all = sb("acc_all", [P, 2, 4 * NB], F32)
        acc = [acc_all[:, k, :] for k in range(2)]
        z = [sb(f"z{k}", [P, NB], F32) for k in range(2)]
        dense = sb("dense", [P, B], F32R)
        dense_f = acc_all[0:D, :, :].rearrange("p k c -> p (k c)")
        y = [sb(f"y{k}", [1, NB], F32) for k in range(2)]
        w1z = sb("w1z", [P, H1], F32)
        w1d = sb("w1d", [P, H1], F32R)
        w2s = sb("w2s", [P, H1 // P, H2], F32)
        w3s = sb("w3s", [P, H2 // P], F32)
        b1s = sb("b1s", [P, H1 // P], F32)
        b2s = sb("b2s", [P, H2 // P], F32)
        h1 = sb("h1", [P, H1 // P, NB], F32)
        w1d_f = h1[0:D, 0:2, :].rearrange("p k c -> p (k c)")
        h2 = sb("h2", [P, H2 // P, NB], F32)

        delta = [pb(f"delta{k}", [P, 4 * NB], F32) for k in range(2)]
        turned = [pb(f"turned{k}", [P, 2, 2, TB], F32) for k in range(2)]
        side = [pb(f"side{k}", [P, 512], F32) for k in range(2)]

        idx_in = [sem(f"idx_in{k}") for k in range(4)]
        gathered = [sem(f"gathered{k}") for k in range(4)]
        idb_in = sem("idb_in")
        tables_in = [sem(f"tables_in{k}") for k in range(PAIRS)]
        wj_in = sem("wj_in")
        mlp_in = sem("mlp_in")
        rest_in = sem("rest_in")
        stored = [sem(f"stored{k}") for k in range(2)]
        pads_zero = sem("pads_zero")
        ones_set = sem("ones_set")
        wj_zero = sem("wj_zero")
        dense_zero = sem("dense_zero")
        ident_set = sem("ident_set")
        rows_set = sem("rows_set")
        part1 = sem("part1")
        rest1 = sem("rest1")
        part2 = sem("part2")
        split = sem("split")
        cast = sem("cast")
        hot = sem("hot")
        looked = sem("looked")
        filled = sem("filled")
        turned_up = sem("turned_up")
        xh_ready = sem("xh_ready")
        xl_ready = sem("xl_ready")
        dense_high = sem("dense_high")
        dense_low = sem("dense_low")
        wj_high = sem("wj_high")
        wj_low = sem("wj_low")
        projected = sem("projected")
        squared = sem("squared")
        summed = sem("summed")
        z_ready = sem("z_ready")
        mlp_done = sem("mlp_done")
        mlp_read = sem("mlp_read")

        out_row = out.rearrange("b o -> o b")
        GATHERS = F - N_ONEHOT
        at_units = lambda s: s * UNITS
        at_quads = lambda s: s * QUADS
        at_sums = lambda s: s * (QUADS - 1)
        at_looks = lambda s: (s + 1) * LOOKS
        at_pairs = lambda s: (s + 1) * PAIRS
        at_mlps = lambda s: (s - 1) * 4
        at_reads = lambda s: (s - 1) * MLPS

        def wait(eng, semaphore, value):
            if not isinstance(value, int) or value > 0:
                eng.wait_ge(semaphore, value)

        def supersteps(eng, step, first, last):
            assert (last - first) % 2 == 1
            with eng.Fori(0, (last - first + 1) // 2) as i:
                for k in range(2):
                    step(i * 2 + (first + k), (first + k) % 2)

        with nc.Block() as block:

            @block.sync
            def _(sp):
                def load_idx(s, k):
                    sp.dma_start(idx[k][:, :], ids[bass.ds((s * 2 + k % 2) * TB, TB), :]).then_inc(idx_in[k], 16)

                def load_idb(s):
                    src = ids_by_field[:, bass.ds(s * NB, NB)]
                    sp.dma_start(idb[:, :, :], src.partition_broadcast(KP)).then_inc(idb_in, 16)

                load_idx(0, 0)
                load_idx(0, 1)
                load_idb(0)
                for k, ch in enumerate(PAIR_CH):
                    if k >= STAGES:
                        sp.wait_ge(split, k - STAGES + 1)
                    for q in range(PAIR_Q[k]):
                        sp.dma_start(stage[k][:, q, :, :], tables[2 * k + q].rearrange("(p c) e -> p c e", c=ch)).then_inc(tables_in[k], 16)
                    if k == STAGES - 1:
                        sp.dma_start(dense_f[:, :], dense_t).then_inc(mlp_in, 16)
                        sp.dma_start(w1d_f[:, :], w1[P:P + D, :]).then_inc(mlp_in, 16)
                        sp.wait_ge(wj_zero, J)
                        for j in range(J):
                            sp.dma_start(wj[j][j:KT:J, :], w_t).then_inc(wj_in, 16)
                load_idx(1, 2)
                load_idx(1, 3)
                sp.wait_ge(cast, 2)
                load_idb(1)
                sp.dma_start(w1z[:, :], w1[0:P, :]).then_inc(rest_in, 16)
                sp.dma_start(w2s[:, :, :], w2.rearrange("(k p) n -> p k n", p=P)).then_inc(rest_in, 16)
                with nc.allow_non_contiguous_dma(reason="small vectors, once"):
                    sp.dma_start(w3s[:, :], w3.rearrange("(k p) o -> p (k o)", p=P)).then_inc(rest_in, 16)
                    sp.dma_start(b1s[:, :], b1.rearrange("(k p) -> p k", p=P)).then_inc(stored[0], 16)
                    sp.dma_start(b2s[:, :], b2.rearrange("(k p) -> p k", p=P)).then_inc(stored[1], 16)

                def step(s, p):
                    for k in (2 * p, 2 * p + 1):
                        sp.wait_ge(gathered[k], (s - p) * (8 * GATHERS))
                        load_idx(s, k)
                    sp.wait_ge(cast, s * 2)
                    load_idb(s)

                supersteps(sp, step, 2, STEPS - 1)
                sp.wait_ge(cast, STEPS * 2)
                load_idb(STEPS - 1)
                for k in range(2):
                    sp.wait_ge(stored[k], 16 + 16 * (STEPS // 2))

            @block.gpsimd
            def _(pool):
                def gather(s, p, first=False):
                    if not first:
                        pool.wait_ge(turned_up, at_units(s - 1))
                    for k in (2 * p, 2 * p + 1):
                        pool.wait_ge(idx_in[k], 16 if first else s * 8 + (16 - 8 * p))
                        if not first:
                            pool.nop(nofuse=True)
                        for f in range(N_ONEHOT, F):
                            pool.indirect_dma_start(
                                x_slots[k][:, f, 0:E], None, tables[f],
                                bass.IndirectOffsetOnAxis(idx[k][:, f:f + 1], 0),
                            ).then_inc(gathered[k], 16)

                for ch, rows in row_no.items():
                    pool.iota(rows[:, :], [[1, ch]], base=0, channel_multiplier=ch,
                              allow_small_or_imprecise_dtypes=True).then_inc(rows_set, 1)
                pool.wait_ge(ones_set, 1)
                pool.affine_select(ident[:, :], ones[:, :], [[-1, P]], ALU.is_equal, 0.0,
                                   base=0, channel_multiplier=1).then_inc(ident_set, 1)
                gather(0, 0, first=True)
                pool.wait_ge(split, PAIRS)
                gather(1, 1, first=True)
                supersteps(pool, gather, 2, STEPS - 1)

            @block.tensor
            def _(pe):
                def free_bank(s, n):
                    known = isinstance(s, int)
                    for back in range(3):
                        for m in reversed(range(n if back == 0 else len(JOBS))):
                            kind, what = JOBS[m][:2]
                            there = not known or (s - back >= 1 if kind == "mlp" else -1 <= s - back < STEPS - 1)
                            if m % 2 == n % 2 and there:
                                if kind == "look":
                                    pe.wait_ge(filled, at_looks(s - back) + 2 * what[0] + what[1] + 1)
                                else:
                                    pe.wait_ge(mlp_read, at_reads(s - back) + MLP_READS[what])
                                return

                def look_up(s, n, k, h):
                    free_bank(s, n)
                    if h == 0:
                        pe.wait_ge(hot, at_pairs(s) + k + 1)
                    if isinstance(s, int) and s == -1 and h == 0:
                        pe.wait_ge(split, k + 1)
                    for q in range(PAIR_Q[k]):
                        for c in range(PAIR_CH[k]):
                            mm = pe.matmul(side[n % 2][:, q * PARTS * E:(q + 1) * PARTS * E],
                                           onehot[k % OHR][:, c, q, h * TB:(h + 1) * TB],
                                           table[k][:, q, c, :, :].rearrange("p r e -> p (r e)"),
                                           start=c == 0, stop=c == PAIR_CH[k] - 1)
                    mm.then_inc(looked, 1)

                def mlp(s, n, part, p):
                    if part == 0:
                        pe.wait_ge(z_ready, s)
                    else:
                        pe.wait_ge(mlp_read, at_reads(s) + MLP_READS[part - 1])
                    free_bank(s, n)
                    bank = side[n % 2]
                    if part < 2:
                        for m in range(2):
                            cols = slice((2 * part + m) * P, (2 * part + m + 1) * P)
                            o = bank[:, m * NB:(m + 1) * NB]
                            pe.matmul(o, w1z[:, cols], z[1 - p][:, :], start=True, stop=False)
                            mm = pe.matmul(o, w1d[:, cols], dense[:, bass.ds((s - 1) * NB, NB)],
                                           start=False, stop=True)
                    elif part == 2:
                        for m in range(2):
                            for k in range(H1 // P):
                                mm = pe.matmul(bank[:, m * NB:(m + 1) * NB], w2s[:, k, m * P:(m + 1) * P],
                                               h1[:, k, :], start=k == 0, stop=k == H1 // P - 1)
                    else:
                        for k in range(H2 // P):
                            mm = pe.matmul(bank[0:1, 0:NB], w3s[:, k:k + 1], h2[:, k, :],
                                           start=k == 0, stop=k == H2 // P - 1)
                    mm.then_inc(mlp_done, 1)

                def transpose(s, u, p):
                    if u == 0:
                        for k in (2 * p, 2 * p + 1):
                            pe.wait_ge(gathered[k], (s - p) * (8 * GATHERS) + 16 * GATHERS)
                        pe.wait_ge(filled, at_looks(s))
                    wait(pe, xl_ready, at_units(s) + (u - 1 if u >= 2 else 0))
                    for g in range(2):
                        for h in range(2):
                            e0 = 2 * u + g
                            mm = pe.transpose(turned[u % 2][0:KT, g, h, :], x[2 * p + h][:, e0:e0 + EG * (KT - 1) + 1:EG],
                                              ident[:, :])
                    mm.then_inc(turned_up, 1)

                def project(s, group):
                    u, g = group // 2, group % 2
                    if g == 0:
                        pe.wait_ge(xl_ready, at_units(s) + u + 1)
                    for n in range(len(ORDER)):
                        if ORDER[n][:2] != (u, g):
                            continue
                        j = ORDER[n][2]
                        quad = n // 4
                        if n % 4 == 0:
                            wait(pe, squared, at_quads(s) + quad - 1)
                        o = delta[quad % 2][:, (n % 4) * NB:(n % 4 + 1) * NB]
                        pe.matmul(o, wjh[j][:, :], xh[:, u % XR, g, :], start=True, stop=False)
                        pe.matmul(o, wjh[j][:, :], xl[:, u % XR, g, :], start=False, stop=False)
                        mm = pe.matmul(o, wjl[j][:, :], xh[:, u % XR, g, :], start=False, stop=True)
                        if n % 4 == 3:
                            mm.then_inc(projected, 1)

                def step(s, p, look=True, run_mlp=True):
                    for call in timetable(
                        *[(TURN_AT[u] + 0.2, lambda u=u: transpose(s, u, p)) for u in range(UNITS)],
                        *[(g, lambda g=g: project(s, g)) for g in range(EG)],
                        *[(at + 0.4, lambda n=n, what=what: look_up(s, n, *what))
                          for n, (kind, what, at) in enumerate(JOBS) if kind == "look" and look],
                        *[(at + 0.4, lambda n=n, what=what: mlp(s, n, what, p))
                          for n, (kind, what, at) in enumerate(JOBS) if kind == "mlp" and run_mlp],
                    ):
                        call()

                pe.wait_ge(ident_set, 1)
                for n, (kind, what, _) in enumerate(JOBS):
                    if kind == "look":
                        look_up(-1, n, *what)
                pe.wait_ge(pads_zero, 4)
                pe.wait_ge(wj_low, J)
                step(0, 0, run_mlp=False)
                pe.wait_ge(dense_low, 4)
                pe.wait_ge(rest_in, 16 * 3)
                supersteps(pe, step, 1, STEPS - 2)
                step(STEPS - 1, 1, look=False)
                for n, (kind, what, _) in enumerate(JOBS):
                    if kind == "mlp":
                        mlp(STEPS, n, what, 0)

            @block.scalar
            def _(act):
                def cast_ids(s, half):
                    cols = slice(0, 4) if half == 0 else slice(4, N_ONEHOT)
                    if half == 0:
                        act.wait_ge(idb_in, s * 16 + 16)
                        wait(act, hot, at_pairs(s - 1))
                    act.activation(idh[:, cols, :], idb[:, cols, :], ACT.Copy).then_inc(cast, 1)

                def free_xr(s, u):
                    last = u - XR if u >= XR else LAST_IN_RING(UNITS, XR, u % XR)
                    wait(act, projected, at_quads(s if u >= XR else s - 1) + (FIRST_OF_UNIT[last + 1] - 1) // 4 + 1)

                def high_half(s, u):
                    act.wait_ge(turned_up, at_units(s) + u + 1)
                    free_xr(s, u)
                    act.activation(xh[:, u % XR, :, :], turned[u % 2][0:KT, :, :, :].rearrange("p g h b -> p g (h b)"),
                                   ACT.Copy).then_inc(xh_ready, 1)

                def square(s, quad, p):
                    act.wait_ge(projected, at_quads(s) + quad + 1)
                    if quad == 0:
                        to = acc[p]
                    else:
                        wait(act, summed, at_sums(s) + quad - 1 - (SQ - 1))
                        to = sq[(quad - 1) % SQ]
                    act.activation(to[:, :], delta[quad % 2][:, :], ACT.Square).then_inc(squared, 1)

                def read_mlp(s, n, part, p):
                    act.wait_ge(mlp_done, at_mlps(s) + part + 1)
                    bank = side[n % 2]
                    if part < 3:
                        to, bias = ((h1, b1s), (h1, b1s), (h2, b2s))[part]
                        for m in range(2):
                            k = 2 * part + m if part < 2 else m
                            act.activation(to[:, k, :], bank[:, m * NB:(m + 1) * NB], ACT.Relu,
                                           bias=bias[:, k:k + 1]).then_inc(mlp_read, 1)
                    else:
                        act.wait_ge(stored[1 - p], s * 8 + 8 * p)
                        act.activation(y[1 - p][:, :], bank[0:1, 0:NB], ACT.Copy).then_inc(mlp_read, 1)
                        act.wait_ge(mlp_read, at_reads(s) + MLPS)
                        act.dma_start(out_row[:, bass.ds((s - 1) * NB, NB)], y[1 - p][:, :]).then_inc(stored[1 - p], 16)

                def step(s, p, look=True, run_mlp=True):
                    for call in timetable(
                        *[(TURN_AT[u] + 0.3, lambda u=u: high_half(s, u)) for u in range(UNITS)],
                        *[(QUAD_AT[q] + 0.1, lambda q=q: square(s, q, p)) for q in range(QUADS)],
                        *[(at + 0.6, lambda n=n, what=what: read_mlp(s, n, what, p))
                          for n, (kind, what, at) in enumerate(JOBS) if kind == "mlp" and run_mlp],
                        *[(CAST_AT + 0.1 * half, lambda half=half: cast_ids(s + 2, half)) for half in range(2) if look],
                    ):
                        call()

                cast_ids(0, 0)
                cast_ids(0, 1)
                for k in range(PAIRS + 1):
                    if k < PAIRS:
                        act.wait_ge(tables_in[k], 16 * PAIR_Q[k])
                        act.activation(table[k][:, :, :, 0, :], stage[k], ACT.Copy).then_inc(part1, 1)
                    if k:
                        act.wait_ge(rest1, k)
                        act.activation(table[k - 1][:, :, :, 1, :], stage[k - 1], ACT.Copy).then_inc(part2, 1)
                    if k == STAGES - 1:
                        act.wait_ge(wj_in, 16 * J)
                        for j in range(J):
                            act.activation(wjh[j][:, :], wj[j][:, :], ACT.Copy).then_inc(wj_high, 1)
                        act.wait_ge(mlp_in, 32)
                        act.wait_ge(dense_zero, 2)
                        act.activation(dense[0:D, :], dense_f[:, :], ACT.Copy).then_inc(dense_high, 1)
                        act.activation(dense[64:64 + D, :], dense_f[:, :], ACT.Copy).then_inc(dense_high, 1)
                        act.activation(w1d[0:D, :], w1d_f[:, :], ACT.Copy).then_inc(dense_high, 1)
                        act.activation(w1d[32:32 + D, :], w1d_f[:, :], ACT.Copy).then_inc(dense_high, 1)
                cast_ids(1, 0)
                cast_ids(1, 1)
                step(0, 0, run_mlp=False)
                for k in range(2):
                    act.wait_ge(stored[k], 16)
                supersteps(act, step, 1, STEPS - 2)
                step(STEPS - 1, 1, look=False)
                for n, (kind, what, _) in enumerate(JOBS):
                    if kind == "mlp":
                        read_mlp(STEPS, n, what, 0)

            @block.vector
            def _(dve):
                def make_hot(s, k):
                    dve.wait_ge(cast, (s + 1) * 2 + (1 if 2 * k + 2 <= 4 else 2))
                    if k >= OHR:
                        dve.wait_ge(looked, at_looks(s) + 2 * (k - OHR) + 2)
                    elif not (isinstance(s, int) and s == -1):
                        dve.wait_ge(looked, at_looks(s - 1) + 2 * LAST_IN_RING(PAIRS, OHR, k) + 2)
                    ch = PAIR_CH[k]
                    for c in range(ch):
                        ins = dve.tensor_scalar(onehot[k % OHR][:, c, 0:PAIR_Q[k], :], idh[:, 2 * k:2 * k + PAIR_Q[k], :],
                                                row_no[ch][:, c:c + 1], None, ALU.is_equal)
                    ins.then_inc(hot, 1)

                def low_half(s, u):
                    dve.wait_ge(xh_ready, at_units(s) + u + 1)
                    dve.tensor_tensor(xl[:, u % XR, :, :], turned[u % 2][0:KT, :, :, :].rearrange("p g h b -> p g (h b)"),
                                      xh[:, u % XR, :, :].bitcast(F32), ALU.subtract).then_inc(xl_ready, 1)

                def fill(s, n, k, h, p):
                    dve.wait_ge(looked, at_looks(s) + 2 * k + h + 1)
                    parts = side[n % 2][:, 0:PAIR_Q[k] * PARTS * E].rearrange("p (q r e) -> p q e r", q=PAIR_Q[k], r=PARTS)
                    dve.tensor_reduce(x_slots[2 * p + h][:, 2 * k:2 * k + PAIR_Q[k], 0:E], parts, AX.X, ALU.add).then_inc(filled, 1)

                def add(s, quad, p):
                    if quad == 0:
                        return
                    dve.wait_ge(squared, at_quads(s) + quad + 1)
                    if quad > 1:
                        dve.wait_ge(summed, at_sums(s) + quad - 1)
                    dve.tensor_tensor(acc[p][:, :], acc[p][:, :], sq[(quad - 1) % SQ][:, :], ALU.add).then_inc(summed, 1)
                    if quad == QUADS - 1:
                        dve.wait_ge(summed, at_sums(s) + quad)
                        dve.tensor_reduce(z[p][:, :], acc[p][:, :].rearrange("p (e b) -> p b e", e=4), AX.X,
                                          ALU.add).then_inc(z_ready, 1)

                def step(s, p, look=True):
                    for call in timetable(
                        *[(TURN_AT[u] + 0.4, lambda u=u: low_half(s, u)) for u in range(UNITS)],
                        *[(QUAD_AT[q] + ADD_LAG, lambda q=q: add(s, q, p)) for q in range(QUADS)],
                        *[(at + 0.9, lambda n=n, what=what: fill(s, n, *what, 1 - p))
                          for n, (kind, what, at) in enumerate(JOBS) if kind == "look" and look],
                        *[(HOT_AT[k], lambda k=k: make_hot(s + 1 if k in EARLY else s, k)) for k in range(PAIRS) if look],
                    ):
                        call()

                dve.memset(ones[:, :], 1.0).then_inc(ones_set, 1)
                for j in range(J):
                    dve.memset(wj[j][:, :], 0.0).then_inc(wj_zero, 1)
                for t in x_slots[0:2]:
                    dve.memset(t[:, :, E:PITCH], 0.0).then_inc(pads_zero, 1)
                dve.memset(w1d[:, :].bitcast(F32), 0.0).then_inc(dense_zero, 1)
                dve.memset(dense[:, :].bitcast(F32), 0.0).then_inc(dense_zero, 1)
                dve.wait_ge(rows_set, len(row_no))
                make_hot(-1, 0)
                make_hot(-1, 1)
                for k in range(PAIRS + 1):
                    if k < PAIRS:
                        dve.wait_ge(part1, k + 1)
                        dve.tensor_tensor(stage[k], stage[k], table[k][:, :, :, 0, :], ALU.subtract).then_inc(rest1, 1)
                    if k:
                        dve.wait_ge(part2, k)
                        dve.tensor_tensor(table[k - 1][:, :, :, 2, :], stage[k - 1], table[k - 1][:, :, :, 1, :],
                                          ALU.subtract).then_inc(split, 1)
                dve.wait_ge(split, PAIRS)
                for t in x_slots[2:4]:
                    dve.memset(t[:, :, E:PITCH], 0.0).then_inc(pads_zero, 1)
                dve.wait_ge(wj_high, J)
                for j in range(J):
                    dve.tensor_tensor(wjl[j][:, :], wj[j][:, :], wjh[j][:, :].bitcast(F32), ALU.subtract).then_inc(wj_low, 1)
                for n, (kind, what, _) in enumerate(JOBS):
                    if kind == "look":
                        k, h = what
                        fill(-1, n, k, h, 0)
                        if h == 1 and k + 2 < PAIRS:
                            make_hot(-1, k + 2)
                dve.wait_ge(dense_high, 4)
                for to in (dense[32:32 + D, :], dense[96:96 + D, :]):
                    dve.tensor_tensor(to, dense_f[:, :], dense[0:D, :].bitcast(F32), ALU.subtract).then_inc(dense_low, 1)
                for to in (w1d[64:64 + D, :], w1d[96:96 + D, :]):
                    dve.tensor_tensor(to, w1d_f[:, :], w1d[0:D, :].bitcast(F32), ALU.subtract).then_inc(dense_low, 1)
                for k in EARLY:
                    make_hot(0, k)
                step(0, 0)
                supersteps(dve, step, 1, STEPS - 2)
                step(STEPS - 1, 1, look=False)


def kernel(**inputs):
    import concourse.bacc as bacc
    from concourse.bass_utils import run_bass_kernel_spmd as run

    nc = bacc.Bacc("TRN2", target_bir_lowering=False, num_devices=1)
    arrays = {}

    def put(name, a):
        a = np.ascontiguousarray(a)
        arrays[name] = a
        return nc.dram_tensor(name, a.shape, mybir.dt.from_np(a.dtype), kind="ExternalInput").ap()

    small = []
    for ch, q in zip(PAIR_CH, PAIR_Q):
        small += [f for f in range(F) if inputs[f"tbl_{f}"].shape[0] == KP * ch and f not in small][:q]
    slots = small + [f for f in range(F) if f not in small]
    ids = np.asarray(inputs["ids"])
    tables = [put(f"tbl_{f}", inputs[f"tbl_{f}"]) for f in slots]
    args = [
        put("ids", ids[:, slots]),
        put("ids_by_field", ids[:, small].T),
        put("dense_t", np.asarray(inputs["dense_ctx"]).T),
        put("w_t", np.asarray(inputs["L0_rec_inner_w"])[:, slots].T),
    ]
    args += [put(n, inputs[n]) for n in ("W_top1", "b_top1", "W_top2", "b_top2", "W_top3")]
    out = nc.dram_tensor("out", (B, 1), F32, kind="ExternalOutput").ap()
    build(nc, tables, *args, out)
    r = run(nc, [arrays], core_ids=[0])
    return r.results[0]["out"]
```

```python
from contextlib import ExitStack

import concourse.bass as bass
import numpy as np
from concourse import mybir

F32 = mybir.dt.float32
BF16 = mybir.dt.bfloat16
F16 = mybir.dt.float16
F32R = mybir.dt.float32r
I32 = mybir.dt.int32
ALU = mybir.AluOpType
ACT = mybir.ActivationFunctionType
AX = mybir.AxisListType

P = 128
B, F, E, U = 2048, 39, 64, 128
D, H1, H2 = 16, 512, 256
TB = 128
NB = 2 * TB
STEPS = B // NB

KP = 125
PAIR_CH = [8] * 6 + [10]
PAIRS = len(PAIR_CH)
N_ONEHOT = 2 * PAIRS
MAX_CH = max(PAIR_CH)
PARTS = 3

J = 3
EG = 22
PITCH = J * EG
KT = J * F
UNITS = EG // 2
ORDER = [(g // 2, g % 2, j) for g in range(EG) for j in range(J) if g + EG * j < E]
QUADS = len(ORDER) // 4
FIRST_OF_UNIT = [min(n for n, o in enumerate(ORDER) if o[0] == u) for u in range(UNITS)] + [E]
XR = 4
SQ = 3
OHR = 3
STAGES = 4
HALVES = (slice(0, 4), slice(4, N_ONEHOT))

JOBS = [
    ("look", (0, 0), -0.9), ("look", (0, 1), -0.8), ("mlp", 0, 3), ("look", (1, 0), 3.5),
    ("look", (1, 1), 4.5), ("mlp", 1, 6.5), ("look", (2, 0), 7), ("look", (2, 1), 7),
    ("mlp", 2, 9.5), ("look", (3, 0), 10), ("look", (3, 1), 10.5), ("mlp", 3, 11.5),
    ("look", (4, 0), 12), ("look", (4, 1), 12.5), ("look", (5, 0), 13.5), ("look", (5, 1), 13.5),
    ("look", (6, 0), 15.5), ("look", (6, 1), 17),
]
assert len(JOBS) % 2 == 0
START = -4
TURN_AT = [-1.2, -1.2] + [2 * u - 4.3 for u in range(2, UNITS)]
TURN_LAG = 0.2
HIGH_LAG = -0.1
LOW_LAG = 0.5
QUAD_AT = [2 * ORDER[4 * q + 3][0] + ORDER[4 * q + 3][1] for q in range(QUADS)]
SQUARE_LAG = 0.1
ADD_LAG = 0.6
JOB_LAG = 0.4
FILL_LAG = 0.6
READ_LAG = -0.2
HOT_LEAD = 2.7
HOT_AT = [at - HOT_LEAD for kind, what, at in JOBS if kind == "look" and what[1] == 0]
CAST_AT = max(HOT_AT) + 1


def mlp_jobs(s):
    for n, (kind, part, at) in enumerate(JOBS):
        if kind == "mlp":
            yield n, max(at, EG - 0.6) if part >= 2 and isinstance(s, int) and s == STEPS - 1 else at


def last_in_ring(n, ring, slot):
    return max(m for m in range(n) if m % ring == slot)


def timetable(rows, s):
    steps = [(at + k * EG, k, name, n) for k in (-1, 0, 1) for at, name, n in rows(s + k)
             if START <= at + k * EG < START + EG]
    return [step[1:] for step in sorted(steps, key=lambda step: step[0])]


LOOKS = 2 * PAIRS
MLP_READS = [2, 4, 6, 7]
MLPS = MLP_READS[-1]


def build(nc, tables, ids, ids_by_field, dense_t, w_t, w1, b1, w2, b2, w3, out):
    with ExitStack() as ctx:
        def sb(name, shape, dt):
            return ctx.enter_context(nc.sbuf_tensor(name, shape, dt))

        def pb(name, shape, dt):
            return ctx.enter_context(nc.psum_tensor(name, shape, dt))

        def sem(name):
            return ctx.enter_context(nc.semaphore(name))

        x_all = sb("x_all", [P, 4, F * PITCH], F32)
        x = [x_all[:, k, :] for k in range(4)]
        x_slots = [t.rearrange("p (f c) -> p f c", c=PITCH) for t in x]
        stage = [x_all[0:KP, 2:4, :].rearrange("p k c -> p (k c)")[:, k * 2 * MAX_CH * E:][:, 0:2 * ch * E]
                 .rearrange("p (q c e) -> p q c e", q=2, c=ch)
                 for k, ch in [(n % STAGES, ch) for n, ch in enumerate(PAIR_CH)]]
        idx = [sb(f"idx{k}", [P, F], I32) for k in range(4)]
        idb = sb("idb", [KP, N_ONEHOT, NB], I32)
        idh = sb("idh", [KP, N_ONEHOT, NB], F16)
        onehot = [sb(f"onehot{k}", [KP, MAX_CH, 2, NB], BF16) for k in range(OHR)]
        table = [sb(f"table{k}", [KP, 2, ch, PARTS, E], BF16) for k, ch in enumerate(PAIR_CH)]
        row_no = {ch: sb(f"row_no{ch}", [KP, ch], F32) for ch in sorted(set(PAIR_CH))}
        xh = sb("xh", [KT, XR, 2, NB], F32R)
        xl = sb("xl", [KT, XR, 2, NB], F32R)
        wj = [sb(f"wj{j}", [KT, U], F32) for j in range(J)]
        wjh = [sb(f"wjh{j}", [KT, U], F32R) for j in range(J)]
        wjl = [sb(f"wjl{j}", [KT, U], F32R) for j in range(J)]
        ident = sb("ident", [P, P], F32)
        ones = sb("ones", [P, P], F32)
        sq = [sb(f"sq{k}", [P, 4 * NB], F32) for k in range(SQ)]
        acc_all = sb("acc_all", [P, 2, 4 * NB], F32)
        acc = [acc_all[:, k, :] for k in range(2)]
        z = [sb(f"z{k}", [P, NB], F32) for k in range(2)]
        dense = sb("dense", [P, B], F32R)
        dense_f = acc_all[0:D, :, :].rearrange("p k c -> p (k c)")
        y = [sb(f"y{k}", [1, NB], F32) for k in range(2)]
        w1z = sb("w1z", [P, H1], F32)
        w1d = sb("w1d", [P, H1], F32R)
        w2s = sb("w2s", [P, H1 // P, H2], F32)
        w3s = sb("w3s", [P, H2 // P], F32)
        b1s = sb("b1s", [P, H1 // P], F32)
        b2s = sb("b2s", [P, H2 // P], F32)
        h1 = sb("h1", [P, H1 // P, NB], F32)
        w1d_f = h1[0:D, 0:2, :].rearrange("p k c -> p (k c)")
        h2 = sb("h2", [P, H2 // P, NB], F32)

        delta = [pb(f"delta{k}", [P, 4 * NB], F32) for k in range(2)]
        turned = [pb(f"turned{k}", [P, 2, 2, TB], F32) for k in range(2)]
        side = [pb(f"side{k}", [P, 512], F32) for k in range(2)]

        idx_in = [sem(f"idx_in{k}") for k in range(4)]
        gathered = [sem(f"gathered{k}") for k in range(4)]
        idb_in = [sem(f"idb_in{half}") for half in range(2)]
        tables_in = [sem(f"tables_in{k}") for k in range(PAIRS)]
        wj_in = sem("wj_in")
        mlp_in = sem("mlp_in")
        rest_in = sem("rest_in")
        stored = [sem(f"stored{k}") for k in range(2)]
        pads_zero = sem("pads_zero")
        ones_set = sem("ones_set")
        wj_zero = sem("wj_zero")
        dense_zero = sem("dense_zero")
        ident_set = sem("ident_set")
        rows_set = sem("rows_set")
        part1 = sem("part1")
        rest1 = sem("rest1")
        part2 = sem("part2")
        split = sem("split")
        cast = sem("cast")
        hot = sem("hot")
        looked = sem("looked")
        filled = sem("filled")
        turned_up = sem("turned_up")
        xh_ready = sem("xh_ready")
        xl_ready = sem("xl_ready")
        dense_high = sem("dense_high")
        dense_low = sem("dense_low")
        wj_high = sem("wj_high")
        wj_low = sem("wj_low")
        projected = sem("projected")
        squared = sem("squared")
        summed = sem("summed")
        z_ready = sem("z_ready")
        mlp_done = sem("mlp_done")
        mlp_read = sem("mlp_read")

        out_row = out.rearrange("b o -> o b")
        at_units = lambda s: s * UNITS
        at_quads = lambda s: s * QUADS
        at_sums = lambda s: s * (QUADS - 1)
        at_looks = lambda s: (s + 1) * LOOKS
        at_pairs = lambda s: (s + 1) * PAIRS
        at_mlps = lambda s: (s - 1) * 4
        at_reads = lambda s: (s - 1) * MLPS

        def in_range(s, first=0, last=STEPS - 1):
            return not isinstance(s, int) or first <= s <= last

        def wait(eng, semaphore, value):
            if not isinstance(value, int) or value > 0:
                eng.wait_ge(semaphore, value)

        def supersteps(eng, step, first, last):
            assert (last - first) % 2 == 1
            with eng.Fori(0, (last - first + 1) // 2) as i:
                for k in range(2):
                    step(i * 2 + (first + k), (first + k) % 2)

        with nc.Block() as block:

            @block.sync
            def _(sp):
                def load_idx(s, k):
                    sp.dma_start(idx[k][:, :], ids[bass.ds((s * 2 + k % 2) * TB, TB), :]).then_inc(idx_in[k], 16)

                def load_idb(s):
                    for half, fields in enumerate(HALVES):
                        src = ids_by_field[fields, bass.ds(s * NB, NB)]
                        sp.dma_start(idb[:, fields, :], src.partition_broadcast(KP)).then_inc(idb_in[half], 16)

                load_idx(0, 0)
                load_idx(0, 1)
                load_idb(0)
                for k, ch in enumerate(PAIR_CH):
                    if k >= STAGES:
                        sp.wait_ge(split, k - STAGES + 1)
                    for q in range(2):
                        sp.dma_start(stage[k][:, q, :, :], tables[2 * k + q].rearrange("(p c) e -> p c e", c=ch)).then_inc(tables_in[k], 16)
                    if k == STAGES - 1:
                        sp.dma_start(dense_f[:, :], dense_t).then_inc(mlp_in, 16)
                        sp.dma_start(w1d_f[:, :], w1[P:P + D, :]).then_inc(mlp_in, 16)
                        sp.wait_ge(wj_zero, J)
                        for j in range(J):
                            sp.dma_start(wj[j][j:KT:J, :], w_t).then_inc(wj_in, 16)
                load_idx(1, 2)
                load_idx(1, 3)
                sp.wait_ge(cast, 2)
                load_idb(1)
                sp.dma_start(w1z[:, :], w1[0:P, :]).then_inc(rest_in, 16)
                sp.dma_start(w2s[:, :, :], w2.rearrange("(k p) n -> p k n", p=P)).then_inc(rest_in, 16)
                with nc.allow_non_contiguous_dma(reason="small vectors, once"):
                    sp.dma_start(w3s[:, :], w3.rearrange("(k p) o -> p (k o)", p=P)).then_inc(rest_in, 16)
                    sp.dma_start(b1s[:, :], b1.rearrange("(k p) -> p k", p=P)).then_inc(stored[0], 16)
                    sp.dma_start(b2s[:, :], b2.rearrange("(k p) -> p k", p=P)).then_inc(stored[1], 16)

                def step(s, p):
                    for k in (2 * p, 2 * p + 1):
                        sp.wait_ge(gathered[k], (s - p) * (8 * (F - N_ONEHOT)))
                        load_idx(s, k)
                    sp.wait_ge(cast, s * 2)
                    load_idb(s)

                supersteps(sp, step, 2, STEPS - 1)
                sp.wait_ge(cast, STEPS * 2)
                load_idb(STEPS - 1)
                for k in range(2):
                    sp.wait_ge(stored[k], 16 + 16 * (STEPS // 2))

            @block.gpsimd
            def _(pool):
                def gather(s, p, first=False):
                    if not first:
                        pool.wait_ge(turned_up, at_units(s - 1))
                    for k in (2 * p, 2 * p + 1):
                        pool.wait_ge(idx_in[k], 16 if first else s * 8 + (16 - 8 * p))
                        if not first:
                            pool.nop(nofuse=True)
                        for f in range(N_ONEHOT, F):
                            pool.indirect_dma_start(
                                x_slots[k][:, f, 0:E], None, tables[f],
                                bass.IndirectOffsetOnAxis(idx[k][:, f:f + 1], 0),
                            ).then_inc(gathered[k], 16)

                for ch, rows in row_no.items():
                    pool.iota(rows[:, :], [[1, ch]], base=0, channel_multiplier=ch,
                              allow_small_or_imprecise_dtypes=True).then_inc(rows_set, 1)
                pool.wait_ge(ones_set, 1)
                pool.affine_select(ident[:, :], ones[:, :], [[-1, P]], ALU.is_equal, 0.0,
                                   base=0, channel_multiplier=1).then_inc(ident_set, 1)
                gather(0, 0, first=True)
                pool.wait_ge(split, PAIRS)
                gather(1, 1, first=True)
                supersteps(pool, gather, 2, STEPS - 1)

            @block.tensor
            def _(pe):
                def free_bank(s, n):
                    known = isinstance(s, int)
                    for back in range(3):
                        for m in reversed(range(n if back == 0 else len(JOBS))):
                            kind, what = JOBS[m][:2]
                            there = not known or (s - back >= 1 if kind == "mlp" else -1 <= s - back < STEPS - 1)
                            if m % 2 == n % 2 and there:
                                if kind == "look":
                                    pe.wait_ge(filled, at_looks(s - back) + 2 * what[0] + what[1] + 1)
                                else:
                                    pe.wait_ge(mlp_read, at_reads(s - back) + MLP_READS[what])
                                return

                def look_up(s, n, k, h):
                    free_bank(s, n)
                    if h == 0:
                        pe.wait_ge(hot, at_pairs(s) + k + 1)
                    if isinstance(s, int) and s == -1 and h == 0:
                        pe.wait_ge(split, k + 1)
                    for q in range(2):
                        for c in range(PAIR_CH[k]):
                            mm = pe.matmul(side[n % 2][:, q * PARTS * E:(q + 1) * PARTS * E],
                                           onehot[k % OHR][:, c, q, h * TB:(h + 1) * TB],
                                           table[k][:, q, c, :, :].rearrange("p r e -> p (r e)"),
                                           start=c == 0, stop=c == PAIR_CH[k] - 1)
                    mm.then_inc(looked, 1)

                def mlp(s, n, part, p):
                    if part == 0:
                        pe.wait_ge(z_ready, s)
                    free_bank(s, n)
                    bank = side[n % 2]
                    if part < 2:
                        for m in range(2):
                            cols = slice((2 * part + m) * P, (2 * part + m + 1) * P)
                            o = bank[:, m * NB:(m + 1) * NB]
                            pe.matmul(o, w1z[:, cols], z[1 - p][:, :], start=True, stop=False)
                            mm = pe.matmul(o, w1d[:, cols], dense[:, bass.ds((s - 1) * NB, NB)],
                                           start=False, stop=True)
                    elif part == 2:
                        for m in range(2):
                            for k in range(H1 // P):
                                if m == 0:
                                    pe.wait_ge(mlp_read, at_reads(s) + k + 1)
                                mm = pe.matmul(bank[:, m * NB:(m + 1) * NB], w2s[:, k, m * P:(m + 1) * P],
                                               h1[:, k, :], start=k == 0, stop=k == H1 // P - 1)
                    else:
                        for k in range(H2 // P):
                            pe.wait_ge(mlp_read, at_reads(s) + MLP_READS[1] + k + 1)
                            mm = pe.matmul(bank[0:1, 0:NB], w3s[:, k:k + 1], h2[:, k, :],
                                           start=k == 0, stop=k == H2 // P - 1)
                    mm.then_inc(mlp_done, 1)

                def transpose(s, u, p):
                    if u == 0:
                        for k in (2 * p, 2 * p + 1):
                            pe.wait_ge(gathered[k], (s - p + 2) * (8 * (F - N_ONEHOT)))
                        pe.wait_ge(filled, at_looks(s))
                    wait(pe, xl_ready, at_units(s) + (u - 1 if u >= 2 else 0))
                    for g in range(2):
                        for h in range(2):
                            e0 = 2 * u + g
                            mm = pe.transpose(turned[u % 2][0:KT, g, h, :], x[2 * p + h][:, e0:e0 + EG * (KT - 1) + 1:EG],
                                              ident[:, :])
                    mm.then_inc(turned_up, 1)

                def project(s, group):
                    u, g = group // 2, group % 2
                    if g == 0:
                        pe.wait_ge(xl_ready, at_units(s) + u + 1)
                    for n in range(len(ORDER)):
                        if ORDER[n][:2] != (u, g):
                            continue
                        j = ORDER[n][2]
                        quad = n // 4
                        if n % 4 == 0:
                            wait(pe, squared, at_quads(s) + quad - 1)
                        o = delta[quad % 2][:, (n % 4) * NB:(n % 4 + 1) * NB]
                        pe.matmul(o, wjh[j][:, :], xh[:, u % XR, g, :], start=True, stop=False)
                        pe.matmul(o, wjh[j][:, :], xl[:, u % XR, g, :], start=False, stop=False)
                        mm = pe.matmul(o, wjl[j][:, :], xh[:, u % XR, g, :], start=False, stop=True)
                        if n % 4 == 3:
                            mm.then_inc(projected, 1)

                def rows(s):
                    todo = []
                    if in_range(s):
                        todo += [(TURN_AT[u] + TURN_LAG, "transpose", u) for u in range(UNITS)]
                        todo += [(g, "project", g) for g in range(EG)]
                    if in_range(s, last=STEPS - 2):
                        todo += [(at + JOB_LAG, "look up", n) for n, (kind, _, at) in enumerate(JOBS) if kind == "look"]
                    if in_range(s, first=1, last=STEPS):
                        todo += [(at + JOB_LAG, "mlp", n) for n, at in mlp_jobs(s)]
                    return todo

                def step(s, p):
                    for k, name, n in timetable(rows, s):
                        if name == "transpose":
                            transpose(s + k, n, (p + k) % 2)
                        elif name == "project":
                            project(s + k, n)
                        elif name == "look up":
                            look_up(s + k, n, *JOBS[n][1])
                        else:
                            mlp(s + k, n, JOBS[n][1], (p + k) % 2)

                pe.wait_ge(ident_set, 1)
                for n, (kind, what, _) in enumerate(JOBS):
                    if kind == "look":
                        look_up(-1, n, *what)
                pe.wait_ge(pads_zero, 2)
                pe.wait_ge(wj_low, J)
                step(-1, 1)
                step(0, 0)
                pe.wait_ge(pads_zero, 4)
                pe.wait_ge(dense_low, 4)
                pe.wait_ge(rest_in, 16 * 3)
                supersteps(pe, step, 1, STEPS - 2)
                step(STEPS - 1, 1)
                step(STEPS, 0)

            @block.scalar
            def _(act):
                def cast_ids(s, half):
                    fields = HALVES[half]
                    act.wait_ge(idb_in[half], s * 16 + 16)
                    if half == 0:
                        wait(act, hot, at_pairs(s - 1))
                    act.activation(idh[:, fields, :], idb[:, fields, :], ACT.Copy).then_inc(cast, 1)

                def free_xr(s, u):
                    last = u - XR if u >= XR else last_in_ring(UNITS, XR, u % XR)
                    wait(act, projected, at_quads(s if u >= XR else s - 1) + (FIRST_OF_UNIT[last + 1] - 1) // 4 + 1)

                def high_half(s, u):
                    act.wait_ge(turned_up, at_units(s) + u + 1)
                    free_xr(s, u)
                    act.activation(xh[:, u % XR, :, :], turned[u % 2][0:KT, :, :, :].rearrange("p g h b -> p g (h b)"),
                                   ACT.Copy).then_inc(xh_ready, 1)

                def square(s, quad, p):
                    act.wait_ge(projected, at_quads(s) + quad + 1)
                    if quad == 0:
                        to = acc[p]
                    else:
                        wait(act, summed, at_sums(s) + quad - 1 - (SQ - 1))
                        to = sq[(quad - 1) % SQ]
                    act.activation(to[:, :], delta[quad % 2][:, :], ACT.Square).then_inc(squared, 1)

                def read_mlp(s, n, part, p):
                    act.wait_ge(mlp_done, at_mlps(s) + part + 1)
                    bank = side[n % 2]
                    if part < 3:
                        to, bias = ((h1, b1s), (h1, b1s), (h2, b2s))[part]
                        for m in range(2):
                            k = 2 * part + m if part < 2 else m
                            act.activation(to[:, k, :], bank[:, m * NB:(m + 1) * NB], ACT.Relu,
                                           bias=bias[:, k:k + 1]).then_inc(mlp_read, 1)
                    else:
                        act.wait_ge(stored[1 - p], s * 8 + 8 * p)
                        act.activation(y[1 - p][:, :], bank[0:1, 0:NB], ACT.Copy).then_inc(mlp_read, 1)
                        act.wait_ge(mlp_read, at_reads(s) + MLPS)
                        act.dma_start(out_row[:, bass.ds((s - 1) * NB, NB)], y[1 - p][:, :]).then_inc(stored[1 - p], 16)

                def rows(s):
                    todo = []
                    if in_range(s):
                        todo += [(TURN_AT[u] + HIGH_LAG, "high half", u) for u in range(UNITS)]
                        todo += [(QUAD_AT[q] + SQUARE_LAG, "square", q) for q in range(QUADS)]
                    if in_range(s, first=1, last=STEPS):
                        todo += [(at + JOB_LAG + READ_LAG, "read mlp", n) for n, at in mlp_jobs(s)]
                    if in_range(s, last=STEPS - 2):
                        todo += [(CAST_AT + 0.1 * half, "cast ids", half) for half in range(2)]
                    return todo

                def step(s, p):
                    for k, name, n in timetable(rows, s):
                        if name == "high half":
                            high_half(s + k, n)
                        elif name == "square":
                            square(s + k, n, (p + k) % 2)
                        elif name == "read mlp":
                            read_mlp(s + k, n, JOBS[n][1], (p + k) % 2)
                        else:
                            cast_ids(s + k + 2, n)

                cast_ids(0, 0)
                cast_ids(0, 1)
                for k in range(PAIRS + 1):
                    if k < PAIRS:
                        act.wait_ge(tables_in[k], 32)
                        act.activation(table[k][:, :, :, 0, :], stage[k], ACT.Copy).then_inc(part1, 1)
                    if k:
                        act.wait_ge(rest1, k)
                        act.activation(table[k - 1][:, :, :, 1, :], stage[k - 1], ACT.Copy).then_inc(part2, 1)
                    if k == STAGES - 1:
                        act.wait_ge(wj_in, 16 * J)
                        for j in range(J):
                            act.activation(wjh[j][:, :], wj[j][:, :], ACT.Copy).then_inc(wj_high, 1)
                        act.wait_ge(mlp_in, 32)
                        act.wait_ge(dense_zero, 2)
                        act.activation(dense[0:D, :], dense_f[:, :], ACT.Copy).then_inc(dense_high, 1)
                        act.activation(dense[64:64 + D, :], dense_f[:, :], ACT.Copy).then_inc(dense_high, 1)
                        act.activation(w1d[0:D, :], w1d_f[:, :], ACT.Copy).then_inc(dense_high, 1)
                        act.activation(w1d[32:32 + D, :], w1d_f[:, :], ACT.Copy).then_inc(dense_high, 1)
                act.wait_ge(dense_low, 2)
                act.activation(dense[96:96 + D, :], dense[32:32 + D, :].bitcast(F32), ACT.Copy).then_inc(dense_low, 1)
                act.activation(w1d[96:96 + D, :], w1d[64:64 + D, :].bitcast(F32), ACT.Copy).then_inc(dense_low, 1)
                cast_ids(1, 0)
                cast_ids(1, 1)
                step(-1, 1)
                step(0, 0)
                for k in range(2):
                    act.wait_ge(stored[k], 16)
                supersteps(act, step, 1, STEPS - 2)
                step(STEPS - 1, 1)
                step(STEPS, 0)

            @block.vector
            def _(dve):
                def make_hot(s, k):
                    dve.wait_ge(cast, (s + 1) * 2 + (1 if 2 * k + 2 <= HALVES[0].stop else 2))
                    if k >= OHR:
                        dve.wait_ge(looked, at_looks(s) + 2 * (k - OHR) + 2)
                    elif not (isinstance(s, int) and s == -1):
                        dve.wait_ge(looked, at_looks(s - 1) + 2 * last_in_ring(PAIRS, OHR, k) + 2)
                    ch = PAIR_CH[k]
                    for c in range(ch):
                        ins = dve.tensor_scalar(onehot[k % OHR][:, c, :, :], idh[:, 2 * k:2 * k + 2, :],
                                                row_no[ch][:, c:c + 1], None, ALU.is_equal)
                    ins.then_inc(hot, 1)

                def low_half(s, u):
                    dve.wait_ge(xh_ready, at_units(s) + u + 1)
                    dve.tensor_tensor(xl[:, u % XR, :, :], turned[u % 2][0:KT, :, :, :].rearrange("p g h b -> p g (h b)"),
                                      xh[:, u % XR, :, :].bitcast(F32), ALU.subtract).then_inc(xl_ready, 1)

                def fill(s, n, k, h, p):
                    dve.wait_ge(looked, at_looks(s) + 2 * k + h + 1)
                    parts = side[n % 2][:, 0:2 * PARTS * E].rearrange("p (q r e) -> p q e r", q=2, r=PARTS)
                    dve.tensor_reduce(x_slots[2 * p + h][:, 2 * k:2 * k + 2, 0:E], parts, AX.X, ALU.add).then_inc(filled, 1)

                def add(s, quad, p):
                    if quad == 0:
                        return
                    dve.wait_ge(squared, at_quads(s) + quad + 1)
                    if quad > 1:
                        dve.wait_ge(summed, at_sums(s) + quad - 1)
                    dve.tensor_tensor(acc[p][:, :], acc[p][:, :], sq[(quad - 1) % SQ][:, :], ALU.add).then_inc(summed, 1)
                    if quad == QUADS - 1:
                        dve.wait_ge(summed, at_sums(s) + quad)
                        dve.tensor_reduce(z[p][:, :], acc[p][:, :].rearrange("p (e b) -> p b e", e=4), AX.X,
                                          ALU.add).then_inc(z_ready, 1)

                def rows(s):
                    todo = []
                    if in_range(s):
                        todo += [(TURN_AT[u] + LOW_LAG, "low half", u) for u in range(UNITS)]
                        todo += [(QUAD_AT[q] + ADD_LAG, "add", q) for q in range(QUADS)]
                    if in_range(s, last=STEPS - 2):
                        todo += [(at + FILL_LAG, "fill", n) for n, (kind, _, at) in enumerate(JOBS) if kind == "look"]
                        todo += [(HOT_AT[k], "make hot", k) for k in range(PAIRS)]
                    return todo

                def step(s, p):
                    for k, name, n in timetable(rows, s):
                        if name == "low half":
                            low_half(s + k, n)
                        elif name == "add":
                            add(s + k, n, (p + k) % 2)
                        elif name == "fill":
                            fill(s + k, n, *JOBS[n][1], (p + k + 1) % 2)
                        else:
                            make_hot(s + k, n)

                dve.memset(ones[:, :], 1.0).then_inc(ones_set, 1)
                for j in range(J):
                    dve.memset(wj[j][:, :], 0.0).then_inc(wj_zero, 1)
                for t in x_slots[0:2]:
                    dve.memset(t[:, :, E:PITCH], 0.0).then_inc(pads_zero, 1)
                dve.memset(w1d[:, :].bitcast(F32), 0.0).then_inc(dense_zero, 1)
                dve.memset(dense[:, :].bitcast(F32), 0.0).then_inc(dense_zero, 1)
                dve.wait_ge(rows_set, len(row_no))
                make_hot(-1, 0)
                make_hot(-1, 1)

                def fill_first(pair):
                    for n, (kind, what, _) in enumerate(JOBS):
                        if kind == "look" and what[0] == pair:
                            fill(-1, n, *what, 0)

                for k in range(PAIRS + 1):
                    if k < PAIRS:
                        dve.wait_ge(part1, k + 1)
                        dve.tensor_tensor(stage[k], stage[k], table[k][:, :, :, 0, :], ALU.subtract).then_inc(rest1, 1)
                    if k:
                        dve.wait_ge(part2, k)
                        dve.tensor_tensor(table[k - 1][:, :, :, 2, :], stage[k - 1], table[k - 1][:, :, :, 1, :],
                                          ALU.subtract).then_inc(split, 1)
                    if k == PAIRS - 2:
                        dve.wait_ge(wj_high, J)
                        for j in range(J):
                            dve.tensor_tensor(wjl[j][:, :], wj[j][:, :], wjh[j][:, :].bitcast(F32), ALU.subtract).then_inc(wj_low, 1)
                        dve.wait_ge(dense_high, 4)
                        dve.tensor_tensor(dense[32:32 + D, :], dense_f[:, :], dense[0:D, :].bitcast(F32), ALU.subtract).then_inc(dense_low, 1)
                        dve.tensor_tensor(w1d[64:64 + D, :], w1d_f[:, :], w1d[0:D, :].bitcast(F32), ALU.subtract).then_inc(dense_low, 1)
                    if k >= 2:
                        fill_first(k - 2)
                        if k < PAIRS:
                            make_hot(-1, k)
                fill_first(PAIRS - 1)
                dve.wait_ge(split, PAIRS)
                for t in x_slots[2:4]:
                    dve.memset(t[:, :, E:PITCH], 0.0).then_inc(pads_zero, 1)
                step(-1, 1)
                step(0, 0)
                supersteps(dve, step, 1, STEPS - 2)
                step(STEPS - 1, 1)
                step(STEPS, 0)


def kernel(**inputs):
    import concourse.bacc as bacc
    from concourse.bass_utils import run_bass_kernel_spmd as run

    nc = bacc.Bacc("TRN2", target_bir_lowering=False, num_devices=1)
    arrays = {}

    def put(name, a):
        a = np.ascontiguousarray(a)
        arrays[name] = a
        return nc.dram_tensor(name, a.shape, mybir.dt.from_np(a.dtype), kind="ExternalInput").ap()

    small = []
    for ch in PAIR_CH:
        small += [f for f in range(F) if inputs[f"tbl_{f}"].shape[0] == KP * ch and f not in small][:2]
    slots = small + [f for f in range(F) if f not in small]
    ids = np.asarray(inputs["ids"])
    tables = [put(f"tbl_{f}", inputs[f"tbl_{f}"]) for f in slots]
    args = [
        put("ids", ids[:, slots]),
        put("ids_by_field", ids[:, small].T),
        put("dense_t", np.asarray(inputs["dense_ctx"]).T),
        put("w_t", np.asarray(inputs["L0_rec_inner_w"])[:, slots].T),
    ]
    args += [put(n, inputs[n]) for n in ("W_top1", "b_top1", "W_top2", "b_top2", "W_top3")]
    out = nc.dram_tensor("out", (B, 1), F32, kind="ExternalOutput").ap()
    build(nc, tables, *args, out)
    r = run(nc, [arrays], core_ids=[0])
    return r.results[0]["out"]
```
